# Optimizing a Trainium2 kernel written in Bass

```python
import numpy as np
import jax
import jax.numpy as jnp

def _softmax(x, axis=-1):
    return jax.nn.softmax(x, axis=axis)

def _gelu(x):
    return jax.nn.gelu(x, approximate=True)

def _silu(x):
    return jax.nn.silu(x)

def _sigmoid(x):
    return jax.nn.sigmoid(x)

def _layernorm(x, axis=-1, eps=1e-05):
    m = jnp.mean(x, axis=axis, keepdims=True)
    v = jnp.var(x, axis=axis, keepdims=True)
    return (x - m) / jnp.sqrt(v + eps)

def _scatter_add(tgt, idx, src, axis=0):
    return tgt.at[idx].add(src)

def _segment_sum(src, seg, n):
    return jax.ops.segment_sum(src, seg, n)
kernel_name = 'mk_gnn_preln_d4_gnn_r8_2ea745'

def setup_inputs(seed: int=0):
    np.random.seed(seed)
    _w = jnp.asarray

    def _rec_inputs():
        import jax
        import jax.numpy as jnp
        _gk = jax.random.key(seed)
        x = -0.0005121 + 1.001 * jax.random.normal(jax.random.fold_in(_gk, 1), (12500, 64), jnp.float32)
        _s = jax.random.randint(jax.random.fold_in(_gk, 2), (100000,), 0, 12500, jnp.int32)
        _d = jax.random.randint(jax.random.fold_in(_gk, 3), (100000,), 0, 12500, jnp.int32)
        _loop = jnp.arange(12500, dtype=jnp.int32)
        src = jnp.concatenate([_s, _d, _loop])
        dst = jnp.concatenate([_d, _s, _loop])
        _o = jnp.argsort(dst, stable=True)
        src = src[_o]
        dst = dst[_o]
        edge_attr_64 = 0.000189758 + 1.00013 * jax.random.normal(jax.random.fold_in(_gk, 12), (212500, 64), jnp.float32)
        edge_attr_8 = -4.12889e-05 + 1 * jax.random.normal(jax.random.fold_in(_gk, 13), (212500, 8), jnp.float32)
        edge_type_8 = jax.random.randint(jax.random.fold_in(_gk, 15), (212500,), 0, 8, jnp.int32)
        return (x, src, dst, edge_attr_64, edge_attr_8, edge_type_8)
    x, src, dst, edge_attr_64, edge_attr_8, edge_type_8 = _rec_inputs()

    def _L0_gnn_setup():
        import jax, jax.numpy as jnp
        import numpy as np
        N_NODES = 6250
        N_EDGES = 100000
        NODE_D = 64
        EDGE_D = 64
        HID_D = 128
        key = jax.random.key(seed)
        ks = jax.random.split(key, 8)
        x = jax.random.normal(ks[0], (N_NODES, NODE_D), dtype=jnp.float32)
        edge_index = jax.random.randint(ks[1], (2, N_EDGES), 0, N_NODES, dtype=jnp.int64)
        edge_attr = jax.random.normal(ks[2], (N_EDGES, EDGE_D), dtype=jnp.float32)
        in_d = NODE_D + EDGE_D
        W1 = jax.random.normal(ks[3], (in_d, HID_D), dtype=jnp.float32) / np.sqrt(in_d)
        b1 = jnp.zeros((HID_D,), dtype=jnp.float32)
        W2 = jax.random.normal(ks[4], (HID_D, HID_D), dtype=jnp.float32) / np.sqrt(HID_D)
        b2 = jnp.zeros((HID_D,), dtype=jnp.float32)
        W3 = jax.random.normal(ks[5], (HID_D, NODE_D), dtype=jnp.float32) / np.sqrt(HID_D)
        b3 = jnp.zeros((NODE_D,), dtype=jnp.float32)
        return {'x': x, 'edge_index': edge_index, 'edge_attr': edge_attr, 'W1': W1, 'b1': b1, 'W2': W2, 'b2': b2, 'W3': W3, 'b3': b3}
    _L0_gnn_all = _L0_gnn_setup()
    _L0_gnn_in = {k: v for k, v in _L0_gnn_all.items() if k in ('W1', 'b1', 'W2', 'b2', 'W3', 'b3')}
    del _L0_gnn_all

    def _L1_gnn_setup():
        import jax, jax.numpy as jnp
        import numpy as np
        N_NODES = 12500
        N_EDGES = 160000
        HID = 64
        MSG = 64
        N_ETYPE = 8

        def _ggnn_forward(h, edge_matrix, w_ih, w_hh, b_ih, b_hh, edge_src, edge_dst, edge_type):
            N, H = h.shape
            T = edge_matrix.shape[0]
            M = edge_matrix.shape[1] // H
            A = edge_matrix.reshape(T, M, H)
            Ht = jnp.einsum('tmh,nh->tnm', A, h)
            msg = Ht[edge_type, edge_src]
            m_agg = jax.ops.segment_sum(msg, edge_dst, num_segments=N)
            gi = m_agg @ w_ih.T + b_ih
            gh = h @ w_hh.T + b_hh
            i_r, i_z, i_n = (gi[:, :H], gi[:, H:2 * H], gi[:, 2 * H:])
            h_r, h_z, h_n = (gh[:, :H], gh[:, H:2 * H], gh[:, 2 * H:])
            r = jax.nn.sigmoid(i_r + h_r)
            z = jax.nn.sigmoid(i_z + h_z)
            n = jnp.tanh(i_n + r * h_n)
            return (1.0 - z) * n + z * h
        key = jax.random.key(seed)
        ks = jax.random.split(key, 9)
        s = 1.0 / np.sqrt(HID)
        return {'h': jax.random.normal(ks[0], (N_NODES, HID), jnp.float32) * s, 'edge_matrix': jax.random.normal(ks[1], (N_ETYPE, MSG * HID), jnp.float32) * s, 'w_ih': jax.random.normal(ks[2], (3 * HID, MSG), jnp.float32) * s, 'w_hh': jax.random.normal(ks[3], (3 * HID, HID), jnp.float32) * s, 'b_ih': jax.random.normal(ks[4], (3 * HID,), jnp.float32) * s, 'b_hh': jax.random.normal(ks[5], (3 * HID,), jnp.float32) * s, 'edge_src': jax.random.randint(ks[6], (N_EDGES,), 0, N_NODES, jnp.int32), 'edge_dst': jax.random.randint(ks[7], (N_EDGES,), 0, N_NODES, jnp.int32), 'edge_type': jax.random.randint(ks[8], (N_ETYPE if False else N_EDGES,), 0, N_ETYPE, jnp.int32)}
    _L1_gnn_all = _L1_gnn_setup()
    _L1_gnn_in = {k: v for k, v in _L1_gnn_all.items() if k in ('edge_matrix', 'w_ih', 'w_hh', 'b_ih', 'b_hh')}
    del _L1_gnn_all

    def _L2_gnn_setup():
        import jax, jax.numpy as jnp
        import numpy as np
        N_NODES = 6250
        N_EDGES = 100000
        D = 64
        N_BASIS = 8
        key = jax.random.key(seed)
        ks = jax.random.split(key, 16)
        inp = {'p': jax.random.normal(ks[0], (N_NODES, D), dtype=jnp.float32), 'idx_i': jax.random.randint(ks[1], (N_EDGES,), 0, N_NODES), 'idx_j': jax.random.randint(ks[2], (N_EDGES,), 0, N_NODES), 'basis': jax.random.normal(ks[3], (N_EDGES, N_BASIS), dtype=jnp.float32), 'pp_W1': jax.random.normal(ks[4], (D, D), dtype=jnp.float32) / np.sqrt(D), 'pp_b1': jnp.zeros((D,), dtype=jnp.float32), 'pp_W2': jax.random.normal(ks[5], (D, D), dtype=jnp.float32) / np.sqrt(D), 'pp_b2': jnp.zeros((D,), dtype=jnp.float32), 'pi_W1': jax.random.normal(ks[6], (2 * D, D), dtype=jnp.float32) / np.sqrt(2 * D), 'pi_b1': jnp.zeros((D,), dtype=jnp.float32), 'pi_W2': jax.random.normal(ks[7], (D, D), dtype=jnp.float32) / np.sqrt(D), 'pi_b2': jnp.zeros((D,), dtype=jnp.float32), 'pi_W3': jax.random.normal(ks[8], (D, D * N_BASIS), dtype=jnp.float32) / np.sqrt(D), 'ii_W1': jax.random.normal(ks[9], (D, D), dtype=jnp.float32) / np.sqrt(D), 'ii_b1': jnp.zeros((D,), dtype=jnp.float32), 'ii_W2': jax.random.normal(ks[10], (D, D), dtype=jnp.float32) / np.sqrt(D), 'ii_b2': jnp.zeros((D,), dtype=jnp.float32)}
        return inp
    _L2_gnn_all = _L2_gnn_setup()
    _L2_gnn_in = {k: v for k, v in _L2_gnn_all.items() if k in ('pp_W1', 'pp_b1', 'pp_W2', 'pp_b2', 'pi_W1', 'pi_b1', 'pi_W2', 'pi_b2', 'pi_W3', 'ii_W1', 'ii_b1', 'ii_W2', 'ii_b2')}
    del _L2_gnn_all

    def _L3_gnn_setup():
        import jax, jax.numpy as jnp
        import numpy as np
        N_NODES = 12500

        def _sage_conv(x, edge_index, W_l, b, W_r):
            src, dst = (edge_index[0], edge_index[1])
            msgs = x[src]
            agg = jax.ops.segment_sum(msgs, dst, num_segments=x.shape[0])
            cnt = jax.ops.segment_sum(jnp.ones((edge_index.shape[1],), x.dtype), dst, num_segments=x.shape[0])
            mean = agg / jnp.clip(cnt, 1.0)[:, None]
            return mean @ W_l + b + x @ W_r
        key = jax.random.key(seed)
        ks = jax.random.split(key, 7)
        E = 125000
        x = jax.random.normal(ks[0], (N_NODES, 64), dtype=jnp.float32)
        edge_index = jax.random.randint(ks[1], (2, E), 0, N_NODES, dtype=jnp.int64)
        W1_l = jax.random.normal(ks[2], (64, 128), dtype=jnp.float32) * 0.1
        W1_r = jax.random.normal(ks[3], (64, 128), dtype=jnp.float32) * 0.1
        b1 = jnp.zeros((128,), dtype=jnp.float32)
        W2_l = jax.random.normal(ks[4], (128, 64), dtype=jnp.float32) * 0.1
        W2_r = jax.random.normal(ks[5], (128, 64), dtype=jnp.float32) * 0.1
        b2 = jnp.zeros((64,), dtype=jnp.float32)
        return {'x': x, 'edge_index': edge_index, 'W1_l': W1_l, 'b1': b1, 'W1_r': W1_r, 'W2_l': W2_l, 'b2': b2, 'W2_r': W2_r}
    _L3_gnn_all = _L3_gnn_setup()
    _L3_gnn_in = {k: v for k, v in _L3_gnn_all.items() if k in ('W1_l', 'b1', 'W1_r', 'W2_l', 'b2', 'W2_r')}
    del _L3_gnn_all
    return {'x': x, 'src': src, 'dst': dst, 'edge_attr_64': edge_attr_64, 'edge_attr_8': edge_attr_8, 'edge_type_8': edge_type_8, 'L0_gnn_W1': _L0_gnn_in['W1'], 'L0_gnn_b1': _L0_gnn_in['b1'], 'L0_gnn_W2': _L0_gnn_in['W2'], 'L0_gnn_b2': _L0_gnn_in['b2'], 'L0_gnn_W3': _L0_gnn_in['W3'], 'L0_gnn_b3': _L0_gnn_in['b3'], 'L1_gnn_edge_matrix': _L1_gnn_in['edge_matrix'], 'L1_gnn_w_ih': _L1_gnn_in['w_ih'], 'L1_gnn_w_hh': _L1_gnn_in['w_hh'], 'L1_gnn_b_ih': _L1_gnn_in['b_ih'], 'L1_gnn_b_hh': _L1_gnn_in['b_hh'], 'L2_gnn_pp_W1': _L2_gnn_in['pp_W1'], 'L2_gnn_pp_b1': _L2_gnn_in['pp_b1'], 'L2_gnn_pp_W2': _L2_gnn_in['pp_W2'], 'L2_gnn_pp_b2': _L2_gnn_in['pp_b2'], 'L2_gnn_pi_W1': _L2_gnn_in['pi_W1'], 'L2_gnn_pi_b1': _L2_gnn_in['pi_b1'], 'L2_gnn_pi_W2': _L2_gnn_in['pi_W2'], 'L2_gnn_pi_b2': _L2_gnn_in['pi_b2'], 'L2_gnn_pi_W3': _L2_gnn_in['pi_W3'], 'L2_gnn_ii_W1': _L2_gnn_in['ii_W1'], 'L2_gnn_ii_b1': _L2_gnn_in['ii_b1'], 'L2_gnn_ii_W2': _L2_gnn_in['ii_W2'], 'L2_gnn_ii_b2': _L2_gnn_in['ii_b2'], 'L3_gnn_W1_l': _L3_gnn_in['W1_l'], 'L3_gnn_b1': _L3_gnn_in['b1'], 'L3_gnn_W1_r': _L3_gnn_in['W1_r'], 'L3_gnn_W2_l': _L3_gnn_in['W2_l'], 'L3_gnn_b2': _L3_gnn_in['b2'], 'L3_gnn_W2_r': _L3_gnn_in['W2_r']}

def reference(x, src, dst, edge_attr_64, edge_attr_8, edge_type_8, L0_gnn_W1, L0_gnn_b1, L0_gnn_W2, L0_gnn_b2, L0_gnn_W3, L0_gnn_b3, L1_gnn_edge_matrix, L1_gnn_w_ih, L1_gnn_w_hh, L1_gnn_b_ih, L1_gnn_b_hh, L2_gnn_pp_W1, L2_gnn_pp_b1, L2_gnn_pp_W2, L2_gnn_pp_b2, L2_gnn_pi_W1, L2_gnn_pi_b1, L2_gnn_pi_W2, L2_gnn_pi_b2, L2_gnn_pi_W3, L2_gnn_ii_W1, L2_gnn_ii_b1, L2_gnn_ii_W2, L2_gnn_ii_b2, L3_gnn_W1_l, L3_gnn_b1, L3_gnn_W1_r, L3_gnn_W2_l, L3_gnn_b2, L3_gnn_W2_r):
    import jax
    import jax.numpy as jnp

    def _L0_gnn_ref(x, edge_index, edge_attr, W1, b1, W2, b2, W3, b3):
        import jax, jax.numpy as jnp
        import numpy as np
        N_NODES = 6250
        N_EDGES = 100000
        NODE_D = 64
        EDGE_D = 64
        HID_D = 128
        r = edge_index[1]
        c1ij = jnp.concatenate([x[r], edge_attr], axis=1)
        h = jax.nn.softplus(c1ij @ W1 + b1)
        h = jax.nn.softplus(h @ W2 + b2)
        out = h @ W3 + b3
        agg = jax.ops.segment_sum(out, r, num_segments=x.shape[0])
        return x + agg

    def _L1_gnn_ref(h, edge_matrix, w_ih, w_hh, b_ih, b_hh, edge_src, edge_dst, edge_type):
        import jax, jax.numpy as jnp
        import numpy as np
        N_NODES = 12500
        N_EDGES = 160000
        HID = 64
        MSG = 64
        N_ETYPE = 8

        def _ggnn_forward(h, edge_matrix, w_ih, w_hh, b_ih, b_hh, edge_src, edge_dst, edge_type):
            N, H = h.shape
            T = edge_matrix.shape[0]
            M = edge_matrix.shape[1] // H
            A = edge_matrix.reshape(T, M, H)
            Ht = jnp.einsum('tmh,nh->tnm', A, h)
            msg = Ht[edge_type, edge_src]
            m_agg = jax.ops.segment_sum(msg, edge_dst, num_segments=N)
            gi = m_agg @ w_ih.T + b_ih
            gh = h @ w_hh.T + b_hh
            i_r, i_z, i_n = (gi[:, :H], gi[:, H:2 * H], gi[:, 2 * H:])
            h_r, h_z, h_n = (gh[:, :H], gh[:, H:2 * H], gh[:, 2 * H:])
            r = jax.nn.sigmoid(i_r + h_r)
            z = jax.nn.sigmoid(i_z + h_z)
            n = jnp.tanh(i_n + r * h_n)
            return (1.0 - z) * n + z * h
        return _ggnn_forward(h, edge_matrix, w_ih, w_hh, b_ih, b_hh, edge_src, edge_dst, edge_type)

    def _L2_gnn_ref(p, idx_i, idx_j, basis, pp_W1, pp_b1, pp_W2, pp_b2, pi_W1, pi_b1, pi_W2, pi_b2, pi_W3, ii_W1, ii_b1, ii_W2, ii_b2):
        import jax, jax.numpy as jnp
        import numpy as np
        N_NODES = 6250
        N_EDGES = 100000
        D = 64
        N_BASIS = 8
        p1 = jnp.tanh(p @ pp_W1 + pp_b1) @ pp_W2 + pp_b2
        inter = jnp.concatenate([p1[idx_i], p1[idx_j]], axis=-1)
        inter = inter @ pi_W1 + pi_b1
        inter = inter @ pi_W2 + pi_b2
        inter = inter @ pi_W3
        inter = inter.reshape(inter.shape[0], D, N_BASIS)
        i1 = jnp.einsum('ecb,eb->ec', inter, basis)
        i1 = jnp.tanh(i1 @ ii_W1 + ii_b1) @ ii_W2 + ii_b2
        out = jax.ops.segment_sum(i1, idx_j, num_segments=p1.shape[0])
        return out

    def _L3_gnn_ref(x, edge_index, W1_l, b1, W1_r, W2_l, b2, W2_r):
        import jax, jax.numpy as jnp
        import numpy as np
        N_NODES = 12500

        def _sage_conv(x, edge_index, W_l, b, W_r):
            src, dst = (edge_index[0], edge_index[1])
            msgs = x[src]
            agg = jax.ops.segment_sum(msgs, dst, num_segments=x.shape[0])
            cnt = jax.ops.segment_sum(jnp.ones((edge_index.shape[1],), x.dtype), dst, num_segments=x.shape[0])
            mean = agg / jnp.clip(cnt, 1.0)[:, None]
            return mean @ W_l + b + x @ W_r
        h = jax.nn.relu(_sage_conv(x, edge_index, W1_l, b1, W1_r))
        return _sage_conv(h, edge_index, W2_l, b2, W2_r)
    edge_index = jnp.stack([src, dst])
    h = jnp.maximum(_layernorm(x, axis=-1), 0.0)
    x = x + _L0_gnn_ref(h, edge_index, edge_attr_64, L0_gnn_W1, L0_gnn_b1, L0_gnn_W2, L0_gnn_b2, L0_gnn_W3, L0_gnn_b3)
    h = jnp.maximum(_layernorm(x, axis=-1), 0.0)
    x = x + _L1_gnn_ref(h, L1_gnn_edge_matrix, L1_gnn_w_ih, L1_gnn_w_hh, L1_gnn_b_ih, L1_gnn_b_hh, src, dst, edge_type_8)
    h = jnp.maximum(_layernorm(x, axis=-1), 0.0)
    x = x + _L2_gnn_ref(h, src, dst, edge_attr_8, L2_gnn_pp_W1, L2_gnn_pp_b1, L2_gnn_pp_W2, L2_gnn_pp_b2, L2_gnn_pi_W1, L2_gnn_pi_b1, L2_gnn_pi_W2, L2_gnn_pi_b2, L2_gnn_pi_W3, L2_gnn_ii_W1, L2_gnn_ii_b1, L2_gnn_ii_W2, L2_gnn_ii_b2)
    h = jnp.maximum(_layernorm(x, axis=-1), 0.0)
    x = x + _L3_gnn_ref(h, edge_index, L3_gnn_W1_l, L3_gnn_b1, L3_gnn_W1_r, L3_gnn_W2_l, L3_gnn_b2, L3_gnn_W2_r)
    return x

_drawn_inputs = setup_inputs


def setup_inputs(seed=0):
    import zlib

    import numpy as np

    out = dict(_drawn_inputs(seed))
    spreads = {'L0_gnn_b1': (0.0, 0.268),
     'L0_gnn_b2': (0.0, 0.1),
     'L0_gnn_b3': (0.0, 0.1),
     'L2_gnn_pp_b1': (0.0, 0.275),
     'L2_gnn_pp_b2': (0.0, 0.1),
     'L2_gnn_pi_b1': (0.0, 0.1),
     'L2_gnn_pi_b2': (0.0, 0.1),
     'L2_gnn_ii_b1': (0.0, 0.1),
     'L2_gnn_ii_b2': (0.0, 0.1),
     'L3_gnn_b1': (0.0, 0.8),
     'L3_gnn_b2': (0.0, 0.8)}
    factors = {'L1_gnn_w_hh': 8.0, 'L1_gnn_b_ih': 34.454, 'L1_gnn_b_hh': 36.055}
    for name, (base, spread) in spreads.items():
        noise = np.random.default_rng([zlib.crc32(name.encode()), seed]).standard_normal(out[name].shape)
        drawn = base * np.exp(spread * noise) if base else spread * noise
        out[name] = jnp.asarray(drawn.astype(out[name].dtype))
    for name, factor in factors.items():
        out[name] = (out[name] * factor).astype(out[name].dtype)
    return out
```

```python
import concourse.bass as bass
from concourse import mybir
from contextlib import ExitStack

F32 = mybir.dt.float32
I32 = mybir.dt.int32
BF16 = mybir.dt.bfloat16
ALU = mybir.AluOpType
ACT = mybir.ActivationFunctionType
AX = mybir.AxisListType

P128 = 128
D = 64
H = 128
NT = 8
NBAS = 8
CE = 512
TL = CE // P128
W = 64
RING = 4
GN = 512
GB = GN // P128
EPS = 1e-5
CLIP = 40.0


def build_gnn(nc, t, out, n_nodes, chunks, np_nodes):
    NP, CH = np_nodes, chunks
    ITERS = CH // RING
    NB = NP // P128
    NG = NP // GN
    PASSES = -(-n_nodes // W)
    assert CH % RING == 0 and ITERS >= 3 and NG % 2 == 0 and NP >= n_nodes + W

    ctx = ExitStack()
    with ctx:
        def sb(name, shape, dt=F32):
            return ctx.enter_context(nc.sbuf_tensor(name, shape, dt))

        def sem(name):
            return ctx.enter_context(nc.semaphore(name))

        def dram(name, shape, dt=F32):
            return nc.dram_tensor(name, shape, dt, kind="Internal").ap()

        tab_g = dram("tab_g", [NP, H])
        tab_msg = dram("tab_msg", [NP * NT, D])
        tab_u = dram("tab_u", [NP, D])
        tab_v = dram("tab_v", [NP, D])
        tab_h = dram("tab_h", [NP, D])
        tab_q = dram("tab_q", [NP, D])
        basis_parts = dram("basis_parts", [3, NBAS * CH * CE], BF16)
        bias_parts = dram("bias_parts", [3, H + D], BF16)

        x = sb("x_nodes", [P128, NB, D])
        h = sb("h_nodes", [P128, NB, D])
        acc = sb("acc", [D + 1, NP])
        scr = sb("scr", [P128, NB * D])
        dst_f = sb("dst_f", [P128, CH * TL])
        rel = sb("rel", [P128, CH * TL])
        src_i = sb("src_i", [P128, CH * TL], I32)
        row_i = sb("row_i", [P128, CH * TL], I32)
        first_f = sb("first_f", [P128, CH])
        base_f = sb("base_f", [P128, CH])
        node_of = sb("node_of", [P128, CH])
        base_i = sb("base_i", [1, CH], I32)
        iota_w = sb("iota_w", [P128, W])
        lane_w = sb("lane_w", [P128, 1])
        flag = sb("flag", [P128, 8])
        passes_i = sb("passes_i", [1, 1], I32)
        ident = sb("ident", [P128, P128])
        ones = sb("ones", [P128, P128])
        ones_b = sb("ones_b", [3, P128], BF16)
        eps_c = sb("eps_c", [P128, 1])
        mean = sb("mean", [P128, NB])
        rstd = sb("rstd", [P128, NB])
        cnt = sb("cnt", [P128, NB])
        IS_BAD, IS_FIT, STEP, AT, TMP = (slice(n, n + 1) for n in range(5))


        mov = sb("mov", [P128, RING, CE])
        win = sb("win", [P128, RING, H])
        outs = sb("outs", [P128, GB, GN])
        gat, sel = (outs[:, 2 * n:2 * n + 2, :].rearrange("p a (b k c) -> p (a b) k c", b=2, k=TL) for n in range(2))
        idx = sb("idx", [P128, RING, TL], I32)
        bas = sb("bas", [3 * NBAS, RING, CE], BF16)
        moved = sb("moved", [H, 2, W])
        pair = sb("pair", [3 * NBAS, 4, P128], BF16)
        ring_mem = scr if NB * D >= 11 * CE else sb("ring_mem", [P128, 11 * CE])

        def ring2(n):
            return ring_mem[:, 2 * n * CE:2 * (n + 1) * CE].rearrange("p (s e) -> p s e", s=2)

        soft1, hid1, soft2, hid2 = (ring2(n) for n in range(4))
        zed = ring_mem[:, 0:8 * CE].rearrange("p (s j e) -> p s j e", s=2, j=4)
        inter = ring2(4)
        tan = ring_mem[:, 10 * CE:11 * CE].rearrange("p (s k c) -> p s k c", s=2, k=TL)

        stage_h = mov[:, 0, :].rearrange("p (s k c) -> p s k c", s=2, k=GB)
        stage_a = mov[:, 1:3, :]
        hT = sb("hT", [D + 1, 2, GN])
        tT = sb("tT", [P128, 2, GN])
        gates = ring_mem[:, 0:2 * CE].rearrange("p (s k c) -> p s k c", s=2, k=GB)
        cand = ring_mem[:, 4 * CE:5 * CE].rearrange("p (s k c) -> p s k c", s=2, k=GB)
        delta = ring_mem[:, 5 * CE:6 * CE].rearrange("p (s k c) -> p s k c", s=2, k=GB)
        self_part = ring2(3)
        hidn = ring2(4)

        w_l0n = sb("w_l0n", [D + 1, H])
        w_l0m = sb("w_l0m", [H, H])
        w_l0o = sb("w_l0o", [H, D + 1])
        b_l0o = sb("b_l0o", [P128, D + 1])
        w_typ = sb("w_typ", [D, NT * D])
        w_ih = sb("w_ih", [D, 4 * D])
        w_hh = sb("w_hh", [D + 1, 4 * D])
        w_pp1 = sb("w_pp1", [D + 1, D])
        w_uv = sb("w_uv", [D + 1, 2 * D])
        w_bas = sb("w_bas", [P128, 4, D])
        w_ii2 = sb("w_ii2", [D + 1, D])
        w_c1l = sb("w_c1l", [D, H])
        w_c1r = sb("w_c1r", [D + 1, H])
        w_c2 = sb("w_c2", [H, 2 * D])
        b_c2 = sb("b_c2", [1, 2 * D])
        bpart = sb("bpart", [3, H + D], BF16)
        raw = tT[:, :, :].rearrange("p s e -> p (s e)")
        r_pp2T, r_w1aT, r_w1bT, r_w2, r_iw1 = (raw[0:D, n * D:(n + 1) * D] for n in range(5))
        r_pp2b, r_pib1 = raw[0:D, 5 * D:5 * D + 1], raw[0:D, 5 * D + 1:5 * D + 2]
        r_wab = raw[0:D, 6 * D:8 * D]
        r_pib2 = raw[0:1, 8 * D:9 * D]
        r_b, r_bd = raw[0:1, 9 * D:12 * D], raw[0:1, 12 * D:15 * D]
        r_w3 = outs[0:D, 0, :]
        b_rz = outs[0:D + 1, 2, 0:2 * D]
        r_parts = [outs[0:1, 1, n * 96:(n + 1) * 96].bitcast(BF16) for n in range(3)]

        KPB = NBAS * CH * CE // P128
        PW = max(w for w in range(32, KPB + 1, 32) if KPB % w == 0 and 2 * w <= NB * D and 3 * (w // 2) <= NB * D)
        NPIECE = KPB // PW
        h_flat = h[:, :, :].rearrange("p b c -> p (b c)")
        piece = [h_flat[:, n * PW:(n + 1) * PW] for n in range(2)]
        piece_parts = [scr[:, n * PW // 2:(n + 1) * PW // 2].bitcast(BF16) for n in range(3)]

        ps = ctx.enter_context(nc.psum_tensor("ps", [P128, 8 * 512], F32))

        def bank(n):
            return ps[:, n * 512:(n + 1) * 512]

        loaded = sem("loaded")
        consts = sem("consts")
        flagged = sem("flagged")
        counted = sem("counted")
        folding = sem("folding")
        folded = sem("folded")
        bias_split = sem("bias_split")
        bias_rt = sem("bias_rt")
        piece_in = [sem("piece_in0"), sem("piece_in1")]
        piece_split = sem("piece_split")
        parts_out = sem("parts_out")
        dve_order = sem("dve_order")
        window_order = sem("window_order")
        windowed = sem("windowed")
        normed = sem("normed")
        residual = sem("residual")
        cleared = sem("cleared")
        h_stored = sem("h_stored")
        act_turn = sem("act_turn")
        pool_turn = sem("pool_turn")
        sp_turn = sem("sp_turn")
        pe_turn = sem("pe_turn")
        staged = sem("staged")
        turned = sem("turned")
        lifted = sem("lifted")
        formed = sem("formed")
        shaped = sem("shaped")
        mixed = sem("mixed")
        settled = sem("settled")
        stored = [sem(f"stored{n}") for n in range(GB)]
        win_loaded = [sem(f"win_loaded{n}") for n in range(RING)]
        gathered = [sem(f"gathered{n}") for n in range(RING)]
        idx_ready = sem("idx_ready")
        selT_built = sem("selT_built")
        sel_built = sem("sel_built")
        agg_done = sem("agg_done")
        agg_added = sem("agg_added")
        mm1_done = sem("mm1_done")
        sized1 = sem("sized1")
        softened1 = sem("softened1")
        hid1_ready = sem("hid1_ready")
        mm2_done = sem("mm2_done")
        clipped2 = sem("clipped2")
        softened2 = sem("softened2")
        hid2_ready = sem("hid2_ready")
        hid_summed = sem("hid_summed")
        hid_moved = sem("hid_moved")
        inter_done = sem("inter_done")
        inter_moved = sem("inter_moved")
        bas_spread = sem("bas_spread")
        z_done = sem("z_done")
        pre_done = sem("pre_done")
        tanh_done = sem("tanh_done")

        def done(g, it, u, back=0):
            return g + it * RING + (u + 1 + RING - back)

        def done_of(n, g, it, u, step, back=0):
            return g * n + it * (RING * n) + (u * n + step + 1 + RING * n - back)

        LOOPS = ["T0", "A0", "T1", "A1", "T2", "A2", "A3", "A4"]
        ADDS = {
            "staged": dict(T0=1, A0=1, T1=1, A1=1, T2=1, A2=1, A3=1, A4=1),
            "turned": dict(T0=1, A0=1, T1=1, A1=1, T2=1, A2=0, A3=2, A4=1),
            "lifted": dict(T0=1, A0=0, T1=1, A1=1, T2=1, A2=0, A3=2, A4=0),
            "formed": dict(T0=1, A0=0, T1=4, A1=1, T2=2, A2=1, A3=2, A4=0),
            "shaped": dict(T0=0, A0=0, T1=0, A1=2, T2=1, A2=0, A3=2, A4=0),
            "mixed": dict(T0=0, A0=1, T1=0, A1=5, T2=0, A2=0, A3=1, A4=0),
            "settled": dict(T0=1, A0=1, T1=4, A1=1, T2=1, A2=1, A3=1, A4=1),
        }
        START = dict(settled=8)
        STORES = dict(T0=(2, 1), T1=(4, 1), T2=(2, 2), A3=(2, 1), A4=(2, 1))

        def at(name, loop, grp, n=0, back=0):
            before = START.get(name, 0) + sum(ADDS[name][k] * NG for k in LOOPS[:LOOPS.index(loop)])
            return grp * ADDS[name][loop] + (before - back * ADDS[name][loop] + n + 1)

        def end(name, loop):
            return at(name, loop, NG - 1, ADDS[name][loop] - 1)

        def stores_by(loop, buf):
            total = 1
            for k in LOOPS[:LOOPS.index(loop)] if loop else LOOPS:
                if k in STORES and buf < STORES[k][0]:
                    total += (NG // 2 if STORES[k][0] == 2 else NG) * STORES[k][1]
            return 16 * total

        def wait_stores(eng, loop):
            for n in range(GB):
                eng.wait_ge(stored[n], stores_by(loop, n))

        AFTER = ["A0", "A1", "A2", "A3", "A4"]
        GATHER = {1: 0, 2: 1, 3: 2, 4: 3}
        WINDOW = {0: 0, 2: 1}

        def passes_of(eng):
            eng.wait_ge(counted, 1)
            return eng.value_load(passes_i[0:1, 0:1], min_val=1, max_val=PASSES)

        def bases_of(kind, c):
            return nc.values_load_multi_w_load_instructions(
                base_i[0:1, bass.ds(c, RING)], engines=[kind], min_val=0, max_val=NP - W,
                skip_runtime_bounds_check_because="the starts are clamped when they are computed")[1]

        def chunk_loop(eng, stages, kind=None, base_lag=0):
            last = max(lag for lag, _ in stages)
            peel = max(1, -(-last // RING))

            def starts(it):
                return bases_of(kind, (it - base_lag // RING) * RING) if kind else None

            def step(it, u, which, bases):
                for lag, stage in which:
                    stage(it + (u - lag) // RING, (u - lag) % RING, bases)

            for it in range(peel):
                bases = starts(it) if it * RING >= base_lag else None
                for u in range(RING):
                    step(it, u, [x_ for x_ in stages if it * RING + u >= x_[0]], bases)
            with eng.Fori(peel, ITERS) as it:
                bases = starts(it)
                for u in range(RING):
                    step(it, u, stages, bases)
            for n in range(last):
                if n % RING == 0:
                    bases = starts(ITERS + n // RING)
                step(ITERS + n // RING, n % RING, [x_ for x_ in stages if n < x_[0]], bases)

        INT = I32
        LOADS = [
            (rel[:, :].bitcast(INT), t["dst_em"]), (row_i[:, :], t["typ_em"]), (src_i[:, :], t["src_em"]),
            (base_f[:, :].bitcast(INT), t["dst_first"].to_broadcast([P128, CH])),
            (x[:, :, :], t["x"].rearrange("(b p) c -> p b c", p=P128)),
            (w_l0n[0:D, :], t["L0_W1"][0:D, :]), (w_l0n[D:D + 1, :], t["L0_b1"]), (w_l0m[:, :], t["L0_W2"]),
            (w_l0o[:, 0:D], t["L0_W3"]), (b_l0o[:, 0:D], t["L0_b3"].to_broadcast([P128, D])),
            (w_typ[:, :], t["A_T"]), (w_ih[:, 0:3 * D], t["w_ih_T"]),
            (w_hh[0:D, 0:2 * D], t["w_hh_T"][:, 0:2 * D]), (w_hh[0:D, 3 * D:4 * D], t["w_hh_T"][:, 2 * D:3 * D]),
            (w_hh[D:D + 1, 0:3 * D], t["b_ih"]), (w_hh[D:D + 1, 3 * D:4 * D], t["b_hh"][:, 2 * D:3 * D]),
            (b_rz[D:D + 1, :], t["b_hh"][:, 0:2 * D]),
            (w_pp1[0:D, :], t["pp_W1"]), (w_pp1[D:D + 1, :], t["pp_b1"]),
            (w_ii2[0:D, :], t["ii_W2"]), (w_ii2[D:D + 1, :], t["ii_b2"]),
            (w_c1l[:, :], t["c1_Wl"]), (w_c1r[0:D, :], t["c1_Wr"]), (w_c1r[D:D + 1, :], t["c1_b"]),
            (w_c2[:, 0:D], t["c2_Wl"]), (w_c2[:, D:2 * D], t["c2_Wr"]), (b_c2[:, D:2 * D], t["c2_b"]),
            (r_pp2T, t["pp_W2_T"]), (r_w1aT, t["pi_W1_T"][:, 0:D]), (r_w1bT, t["pi_W1_T"][:, D:2 * D]),
            (r_w2, t["pi_W2"]), (r_iw1, t["ii_W1"]), (r_w3, t["pi_W3_T"]),
            (r_pp2b, t["pp_b2"]), (r_pib1, t["pi_b1"]), (r_pib2, t["pi_b2"]),
            (r_b[:, 0:H], t["L0_b2"]), (r_b[:, H:H + D], t["ii_b1"]),
        ]
        ALL_LOADED = 16 * len(LOADS)
        N_CONSTS = 19

        block = ctx.enter_context(nc.Block())

        @block.sync
        def _(sp):
            for dst, src in LOADS:
                sp.dma_start(dst, src).then_inc(loaded, 16)
            for u in range(RING):
                sp.dma_start(win[0:D, u, :], t["L0_W1"][D:2 * D, :]).then_inc(stored[u], 16)

            for n in range(NPIECE + 1):
                if n < NPIECE:
                    if n >= 2:
                        sp.wait_ge(piece_split, n - 1)
                    sp.dma_start(piece[n % 2], t["ea8_T"][:, n * PW:(n + 1) * PW]).then_inc(piece_in[n % 2], 16)
                if n >= 1:
                    sp.wait_ge(piece_split, n)
                    for a in range(3):
                        sp.dma_start(basis_parts[a, :].rearrange("(p w) -> p w", p=P128)[:, (n - 1) * PW:n * PW],
                                     piece_parts[a]).then_inc(parts_out, 16)
            sp.wait_ge(bias_split, 1)
            for a in range(3):
                sp.dma_start(bias_parts[a:a + 1, :], r_parts[a]).then_inc(bias_rt, 16)
            sp.wait_ge(bias_rt, 48)
            sp.dma_start(bpart[:, :], bias_parts[:, :]).then_inc(bias_rt, 16)

            P = passes_of(sp)

            def store_groups(loop, tables, width):
                with sp.Fori(0, NG // 2) as i:
                    for s in range(2):
                        sp.wait_ge(settled, at("settled", loop, i * 2 + s))
                        rows = outs[:, s, 0:GB * width * len(tables)].rearrange("p (k c) -> p k c", k=GB)
                        for n, table in enumerate(tables):
                            sp.dma_start(
                                table[bass.ds((i * 2 + s) * GN, GN), :].rearrange("(k p) c -> p k c", p=P128),
                                rows[:, :, n * width:(n + 1) * width]).then_inc(stored[s], 16)

            def windows(e, rows, table, width, extra, used):
                wait_stores(sp, AFTER[e])
                with sp.Fori(0, P) as p:
                    gp = sp.snap(p * CH)
                    sp.wait_ge(windowed, P * e + p + 1)
                    sp.sem_inc(sp_turn, 1)
                    with sp.Fori(0, ITERS) as it:
                        base = bases_of(mybir.EngineType.SP, it * RING)
                        for u in range(RING):
                            used(gp, it, u)
                            sp.sem_inc(sp_turn, 1)
                            for dst, src in extra:
                                sp.dma_start(dst[:, u, :], src[:, bass.ds((it * RING + u) * CE, CE)]) \
                                  .then_inc(win_loaded[u], 16)
                            sp.dma_start(mov[rows, u, :].bitcast(I32),
                                         t["dst_row"][:, bass.ds((it * RING + u) * CE, CE)].to_broadcast([D, CE])) \
                              .then_inc(win_loaded[u], 16)
                            sp.dma_start(win[rows, u, 0:width], table[bass.ds(base[u], W), :]) \
                              .then_inc(win_loaded[u], 16)

            def used0(g, it, u):
                sp.wait_ge(mm1_done, done(g, it, u, RING))

            def used2(g, it, u):
                sp.wait_ge(inter_done, done(g, it, u, RING))
                sp.sem_inc(sp_turn, 1)
                sp.wait_ge(bas_spread, done_of(4, g, it, u, 3, 4 * RING))

            store_groups("T0", [tab_g], H)
            windows(0, slice(D, P128), tab_g, H, [(mov[0:D], t["ea64_T"])], used0)

            with sp.Fori(0, NG) as j:
                for k in range(GB):
                    sp.wait_ge(settled, at("settled", "T1", j, k))
                    sp.dma_start(
                        tab_msg[bass.ds((j * GB + k) * (P128 * NT), P128 * NT), :].rearrange("(p t) c -> p (t c)", t=NT),
                        outs[:, k, :]).then_inc(stored[k], 16)

            store_groups("T2", [tab_u, tab_v], D)
            sp.wait_ge(parts_out, 48 * NPIECE)
            windows(2, slice(0, D), tab_v, D, [(bas, basis_parts.rearrange("a (b e) -> (a b) e", b=NBAS))], used2)

            sp.wait_ge(normed, 5 * 4)
            sp.dma_start(tab_h.rearrange("(b p) c -> p b c", p=P128), h[:, :, :]).then_inc(h_stored, 16)
            store_groups("A3", [tab_q], D)
            store_groups("A4", [out], D)
            wait_stores(sp, None)

        @block.gpsimd
        def _(pool):
            made = [0]

            def const(ins):
                made[0] += 1
                ins.then_inc(consts, 1)
                pool.wait_ge(consts, made[0])

            const(nc.gpsimd.memset(ident[:, :], 0.0))
            const(nc.gpsimd.affine_select(out=ident[:, :], in_=ident[:, :], compare_op=ALU.not_equal, fill=1.0, base=0,
                                          pattern=[[-1, P128]], channel_multiplier=1))
            const(nc.gpsimd.memset(pair[:, :, :], 0.0))
            for a in range(3):
                v = pair[:, :, :].rearrange("p j (q c) -> p j q c", q=2)
                const(nc.gpsimd.affine_select(out=v, in_=v, compare_op=ALU.not_equal, fill=1.0, base=-NBAS * a,
                                              pattern=[[-2, 4], [-1, 2], [0, D]], channel_multiplier=1))
            const(nc.gpsimd.iota(iota_w[:, :], pattern=[[1, W]], base=0, channel_multiplier=0,
                                 allow_small_or_imprecise_dtypes=True))
            const(nc.gpsimd.iota(lane_w[:, :], pattern=[[0, 1]], base=0, channel_multiplier=1,
                                 allow_small_or_imprecise_dtypes=True))
            for tile_, value in ((ones[:, :], 1.0), (ones_b[:, :], 1.0), (eps_c[:, :], EPS), (hT[D:D + 1, :, :], 1.0),
                                 (tT[D:D + 1, :, :], 1.0), (w_l0o[:, D:D + 1], 0.0), (b_l0o[:, D:D + 1], 1.0),
                                 (w_ih[:, 3 * D:4 * D], 0.0), (w_hh[0:D, 2 * D:3 * D], 0.0),
                                 (w_uv[D:D + 1, 0:D], 0.0), (b_c2[:, 0:D], 0.0)):
                const(nc.gpsimd.memset(tile_, value))
            assert made[0] == N_CONSTS
            pool.wait_ge(flagged, 1)
            nc.gpsimd.partition_all_reduce(flag[:, IS_BAD], flag[:, TMP], P128, bass.bass_isa.ReduceOp.max) \
                .then_inc(flagged, 1)
            nc.gpsimd.memset(acc[:, :], 0.0).then_inc(cleared, 1)
            P = passes_of(pool)

            pool.wait_ge(normed, 5)
            nc.gpsimd.tensor_tensor(x[:, :, :], x[:, :, :], h[:, :, :], ALU.add).then_inc(residual, 1)

            def clear_acc(loop):
                pool.wait_ge(staged, end("staged", loop))
                nc.gpsimd.memset(acc[0:D, :], 0.0).then_inc(cleared, 1)

            def gather(e, table, free):
                with pool.Fori(0, P) as p:
                    g = pool.snap((P * GATHER[e] + p) * CH)
                    ga = pool.snap((P * e + p) * CH)
                    gi = pool.snap(p * CH)

                    def stage(it, u, _):
                        pool.wait_ge(idx_ready, done(g, it, u))
                        if free is agg_done:
                            pool.wait_ge(agg_done, done(ga, it, u, RING))
                        else:
                            pool.wait_ge(inter_done, done(gi, it, u, RING))
                        pool.sem_inc(pool_turn, 1)
                        for k in range(TL):
                            nc.gpsimd.indirect_dma_start(
                                out=gat[:, u, k, :], out_offset=None, in_=table,
                                in_offset=bass.IndirectOffsetOnAxis(ap=idx[:, u, k:k + 1], axis=0),
                            ).then_inc(gathered[u], 16)

                    chunk_loop(pool, [(0, stage)])

            clear_acc("A0")
            wait_stores(pool, "A1")
            gather(1, tab_msg, agg_done)
            clear_acc("A1")
            wait_stores(pool, "A2")
            gather(2, tab_u, inter_done)
            clear_acc("A2")
            pool.wait_ge(h_stored, 16)
            gather(3, tab_h, agg_done)
            clear_acc("A3")
            wait_stores(pool, "A4")
            gather(4, tab_q, agg_done)

        @block.vector
        def _(dve):
            for s_, n in ((settled, START["settled"]), (idx_ready, RING), (selT_built, RING), (sel_built, RING),
                          (agg_added, RING), (hid1_ready, RING), (clipped2, RING),
                          (hid2_ready, RING), (z_done, 4 * RING)):
                dve.sem_inc(s_, n)
            steps = [0]

            def order(ins):
                steps[0] += 1
                ins.then_inc(dve_order, 1)
                dve.wait_ge(dve_order, steps[0])

            dve.wait_ge(loaded, ALL_LOADED)
            dve.wait_ge(consts, N_CONSTS)

            order(nc.vector.tensor_scalar(flag[:, AT], lane_w[:, :], float(W), -float(W), ALU.is_ge, ALU.mult))
            order(nc.vector.tensor_tensor(lane_w[:, :], lane_w[:, :], flag[:, AT], ALU.add))
            nc.vector.tensor_copy(dst_f[:, :], rel[:, :].bitcast(I32))
            nc.vector.tensor_copy(first_f[:, :], base_f[:, :].bitcast(I32))
            order(nc.vector.scalar_tensor_tensor(out=row_i[:, :], in0=src_i[:, :], scalar=float(NT), in1=row_i[:, :],
                                                 op0=ALU.mult, op1=ALU.add))
            by_chunk = [a[:, :].rearrange("p (c k) -> p c k", k=TL) for a in (rel, dst_f)]
            order(nc.vector.tensor_tensor(by_chunk[0], by_chunk[1],
                                          first_f[:, :].unsqueeze(2).to_broadcast([P128, CH, TL]), ALU.subtract))
            excess = ring_mem[:, 0:CH * TL] if CH * TL <= 11 * CE else scr[:, 0:CH * TL]
            order(nc.vector.scalar_tensor_tensor(out=excess, in0=rel[:, :], scalar=float(W - 1), in1=rel[:, :],
                                                 op0=ALU.subtract, op1=ALU.mult))
            order(nc.vector.scalar_tensor_tensor(out=excess, in0=dst_f[:, :], scalar=0.0, in1=excess,
                                                 op0=ALU.is_ge, op1=ALU.mult))
            nc.vector.tensor_reduce(out=flag[:, TMP], in_=excess, axis=AX.X, op=ALU.max).then_inc(flagged, 1)
            dve.wait_ge(flagged, 2)
            order(nc.vector.tensor_scalar(flag[:, IS_BAD], flag[:, IS_BAD], 0.0, None, ALU.is_gt))
            nc.vector.tensor_scalar(flag[:, IS_FIT], flag[:, IS_BAD], -1.0, 1.0, ALU.mult, ALU.add)
            nc.vector.tensor_scalar(flag[:, STEP], flag[:, IS_BAD], float(W), None, ALU.mult)
            nc.vector.tensor_scalar(passes_i[0:1, :], flag[0:1, IS_BAD], float(PASSES - 1), 1.0, ALU.mult, ALU.add) \
                .then_inc(counted, 1)
            P = passes_of(dve)

            order(nc.vector.tensor_copy(r_parts[0], r_b))
            order(nc.vector.tensor_tensor(r_bd, r_b, r_parts[0], ALU.subtract))
            order(nc.vector.tensor_copy(r_parts[1], r_bd))
            nc.vector.tensor_tensor(r_parts[2], r_bd, r_parts[1], ALU.subtract).then_inc(bias_split, 1)
            nc.vector.tensor_tensor(w_hh[D:D + 1, 0:2 * D], w_hh[D:D + 1, 0:2 * D], b_rz[D:D + 1, :], ALU.add)
            dve.wait_ge(folding, 1)
            nc.vector.tensor_copy(r_wab, bank(0)[0:D, 0:2 * D]).then_inc(folded, 1)
            dve.wait_ge(folding, 2)
            nc.vector.tensor_copy(w_uv[0:D, :], bank(1)[0:D, 0:2 * D])
            nc.vector.tensor_copy(w_uv[D:D + 1, D:2 * D], bank(2)[0:1, 0:D])
            order(nc.vector.tensor_copy(w_bas[:, :, :], bank(3)[:, 0:4 * D].rearrange("p (j c) -> p j c", j=4)))

            for n in range(NPIECE):
                pc = piece[n % 2]
                dve.wait_ge(piece_in[n % 2], 16 * (n // 2 + 1))
                if n >= 1:
                    dve.wait_ge(parts_out, 48 * n)
                order(nc.vector.tensor_copy(piece_parts[0], pc))
                order(nc.vector.tensor_tensor(pc, pc, piece_parts[0], ALU.subtract))
                order(nc.vector.tensor_copy(piece_parts[1], pc))
                nc.vector.tensor_tensor(piece_parts[2], pc, piece_parts[1], ALU.subtract).then_inc(piece_split, 1)
            dve.wait_ge(piece_split, NPIECE)
            dve.wait_ge(parts_out, 48 * NPIECE)

            wide = [P128, NB, D]
            scr_nb = scr[:, :].rearrange("p (b c) -> p b c", b=NB)

            def norm(n):
                order(nc.vector.tensor_reduce(out=mean[:, :], in_=x[:, :, :], axis=AX.X, op=ALU.add))
                order(nc.vector.tensor_scalar(mean[:, :], mean[:, :], 1.0 / D, None, ALU.mult))
                nc.vector.tensor_tensor(h[:, :, :], x[:, :, :], mean[:, :].unsqueeze(2).to_broadcast(wide),
                                        ALU.subtract).then_inc(normed, 1)
                dve.wait_ge(normed, 5 * n + 2)
                nc.vector.tensor_reduce(out=rstd[:, :], in_=scr_nb, axis=AX.X, op=ALU.add).then_inc(normed, 1)
                dve.wait_ge(normed, 5 * n + 4)
                order(nc.vector.reciprocal(rstd[:, :], rstd[:, :]))
                nc.vector.scalar_tensor_tensor(out=h[:, :, :], in0=h[:, :, :], scalar=0.0,
                                               in1=rstd[:, :].unsqueeze(2).to_broadcast(wide),
                                               op0=ALU.max, op1=ALU.mult).then_inc(normed, 1)

            def set_windows(e, p):
                w0 = dve.snap((P * e + p) * 4)
                if e > 0:
                    dve.wait_ge(window_order, w0)
                nc.vector.tensor_scalar(base_f[:, :], first_f[:, :], flag[:, IS_FIT], flag[:, AT], ALU.mult, ALU.add) \
                    .then_inc(window_order, 1)
                dve.wait_ge(window_order, w0 + 1)
                nc.vector.tensor_scalar(base_f[:, :], base_f[:, :], 0.0, float(NP - W), ALU.max, ALU.min) \
                    .then_inc(window_order, 1)
                dve.wait_ge(window_order, w0 + 2)
                nc.vector.tensor_copy(base_i[0:1, :], base_f[0:1, :])
                nc.vector.tensor_scalar(node_of[:, :], base_f[:, :], lane_w[:, 0:1], None, ALU.add)
                nc.vector.tensor_tensor(by_chunk[0], by_chunk[1],
                                        base_f[:, :].unsqueeze(2).to_broadcast([P128, CH, TL]), ALU.subtract) \
                    .then_inc(window_order, 1)
                nc.vector.tensor_tensor(flag[:, AT], flag[:, AT], flag[:, STEP], ALU.add).then_inc(window_order, 1)
                dve.wait_ge(window_order, w0 + 4)
                dve.sem_inc(windowed, 1)

            def edge_phase(e, make):
                order(nc.vector.memset(flag[:, AT], 0.0))
                dve.wait_ge(cleared, e + 1)
                wait_stores(dve, AFTER[e])
                with dve.Fori(0, P) as p:
                    set_windows(e, p)
                    chunk_loop(dve, make(p), mybir.EngineType.DVE, ADD_LAG[e])

            ADD_LAG = {0: 8, 1: 4, 2: 8, 3: 4, 4: 4}

            def add_stage(e, p, rows, banks):
                ga = dve.snap((P * e + p) * CH)

                def stage(it, u, base):
                    dve.wait_ge(agg_done, done(ga, it, u))
                    dve.wait_ge(agg_added, done(ga, it, u, 1))
                    into = acc[0:rows, bass.ds(base[u], W)]
                    nc.vector.tensor_tensor(into, into, bank(banks[u % len(banks)])[0:rows, 0:W], ALU.add) \
                        .then_inc(agg_added, 1)
                return stage

            def sel_stage(e, p):
                ga = dve.snap((P * e + p) * CH)

                def stage(it, u, _):
                    dve.wait_ge(agg_done, done(ga, it, u, RING))
                    at_ = rel[:, bass.ds((it * RING + u) * TL, TL)]
                    nc.vector.tensor_tensor(sel[:, u, :, :], at_.unsqueeze(2).to_broadcast([P128, TL, W]),
                                            iota_w[:, :].unsqueeze(1).to_broadcast([P128, TL, W]), ALU.is_equal) \
                        .then_inc(sel_built, 1)
                return stage

            def selT_stage(e, p, rows, n_loads):
                gw = dve.snap((P * WINDOW[e] + p) * ITERS)

                def stage(it, u, _):
                    dve.wait_ge(win_loaded[u], (gw + it) * (16 * n_loads) + 16 * n_loads)
                    nc.vector.tensor_scalar(mov[rows, u, :], mov[rows, u, :].bitcast(I32),
                                            node_of[rows, bass.ds(it * RING + u, 1)], None, ALU.is_equal) \
                        .then_inc(selT_built, 1)
                return stage

            def idx_stage(e, p, numbers):
                g = dve.snap(p * CH if e == 2 else (P * e + p) * CH)

                def stage(it, u, _):
                    dve.wait_ge(inter_done if e == 2 else agg_done, done(g, it, u, RING))
                    nc.vector.tensor_scalar(idx[:, u, :], numbers[:, bass.ds((it * RING + u) * TL, TL)], 0.0, None,
                                            ALU.add).then_inc(idx_ready, 1)
                return stage

            def edge_mlp(p):
                g = dve.snap(p * CH)

                def soft(ready, softened, used, clip_src, soft_buf, hid_buf, bank0):
                    def stage(it, u, _):
                        dve.wait_ge(softened, done_of(2, g, it, u, 1))
                        dve.wait_ge(used, done(g, it, u, 2))
                        nc.vector.tensor_tensor(hid_buf[:, u % 2, :], bank(bank0 + u % 2), soft_buf[:, u % 2, :],
                                                ALU.max).then_inc(ready, 1)
                    return stage

                def clip(made, ready, clipped, soft_buf, bank0):
                    def stage(it, u, _):
                        dve.wait_ge(made, done(g, it, u))
                        dve.wait_ge(ready, done(g, it, u, 2))
                        nc.vector.tensor_scalar(soft_buf[:, u % 2, :], bank(bank0 + u % 2), CLIP, None, ALU.min) \
                            .then_inc(clipped, 1)
                    return stage

                def soft_of_size(it, u, _):
                    dve.wait_ge(softened1, done_of(2, g, it, u, 1))
                    dve.wait_ge(mm2_done, done(g, it, u, 2))
                    nc.vector.scalar_tensor_tensor(out=hid1[:, u % 2, :], in0=bank(u % 2), scalar=0.0,
                                                   in1=soft1[:, u % 2, :], op0=ALU.max, op1=ALU.add) \
                        .then_inc(hid1_ready, 1)

                return [(3, soft_of_size),
                        (5, soft(hid2_ready, softened2, hid_summed, None, soft2, hid2, 2)),
                        (4, clip(mm2_done, hid2_ready, clipped2, soft2, 2)),
                        (0, selT_stage(0, p, slice(D, P128), 3)),
                        (4, sel_stage(0, p)),
                        (8, add_stage(0, p, D + 1, (6, 7)))]

            def interaction(p):
                g = dve.snap(p * CH)

                def z_stage(it, u, _):
                    dve.wait_ge(inter_moved, done(g, it, u))
                    dve.wait_ge(pre_done, done(g, it, u, 2))
                    for j in range(4):
                        dve.wait_ge(bas_spread, done_of(4, g, it, u, j))
                        nc.vector.tensor_tensor(zed[:, u % 2, j, :], bank(2 + j % 2), inter[:, u % 2, :],
                                                ALU.mult).then_inc(z_done, 1)

                return [(0, idx_stage(2, p, src_i)),
                        (2, selT_stage(2, p, slice(0, D), 3)),
                        (4, z_stage),
                        (5, sel_stage(2, p)),
                        (8, add_stage(2, p, D, (6, 7)))]

            def plain(e, numbers):
                return lambda p: [(0, idx_stage(e, p, numbers)), (2, sel_stage(e, p)),
                                  (4, add_stage(e, p, D, (4, 5, 6, 7)))]

            def node_loop(loop, body, n_steps=1):
                with dve.Fori(0, NG // 2) as i:
                    for n in range(n_steps):
                        for s in range(2):
                            body(n, i * 2 + s, s, i)

            def free_outs(loop, i, buf):
                dve.wait_ge(stored[buf], i * (16 * STORES[loop][1]) + stores_by(loop, buf))

            def blocks(j):
                return bass.ds(j * GB, GB)

            norm(0)

            def t0(n, j, s, i):
                dve.wait_ge(formed, at("formed", "T0", j))
                free_outs("T0", i, s)
                nc.vector.tensor_copy(outs[:, s, :], bank(2 + s)).then_inc(settled, 1)

            node_loop("T0", t0)
            edge_phase(0, edge_mlp)

            dve.wait_ge(residual, 1)

            def a0(n, j, s, i):
                dve.wait_ge(turned, at("turned", "A0", j))
                v = bank(s).rearrange("p (k c) -> p k c", k=GB)
                nc.vector.tensor_scalar(cnt[:, blocks(j)], v[:, :, D], 1.0, None, ALU.max).then_inc(mixed, 1)
                nc.vector.tensor_tensor(x[:, blocks(j), :], x[:, blocks(j), :], v[:, :, 0:D], ALU.add) \
                    .then_inc(settled, 1)

            node_loop("A0", a0)
            dve.wait_ge(settled, end("settled", "A0"))
            order(nc.vector.reciprocal(cnt[:, :], cnt[:, :]))

            norm(1)
            with dve.Fori(0, NG // 2) as i:
                for s in range(2):
                    for k in range(GB):
                        dve.wait_ge(formed, at("formed", "T1", i * 2 + s, k))
                        dve.wait_ge(stored[k], (i * 2 + s) * 16 + stores_by("T1", k))
                        nc.vector.tensor_copy(outs[:, k, :], bank(2 + k)).then_inc(settled, 1)
            edge_phase(1, plain(1, row_i))

            def a1(n, j, s, i):
                v = ps[:, (2 + 2 * s) * 512:(4 + 2 * s) * 512].rearrange("p (k c) -> p k c", k=GB)
                if n == 0:
                    dve.wait_ge(shaped, at("shaped", "A1", j - s, s))
                    nc.vector.tensor_tensor(cand[:, s], gates[:, s, :, 0:D], v[:, :, 3 * D:4 * D], ALU.mult) \
                        .then_inc(mixed, 1)
                if n == 1:
                    dve.wait_ge(mixed, at("mixed", "A1", j - s, s))
                    nc.vector.tensor_tensor(cand[:, s], cand[:, s], v[:, :, 2 * D:3 * D], ALU.add).then_inc(mixed, 1)
                if n == 2:
                    dve.wait_ge(shaped, at("shaped", "A1", j - s, 2 + s))
                    nc.vector.tensor_tensor(delta[:, s], stage_h[:, s], cand[:, s], ALU.subtract).then_inc(mixed, 1)
                if n == 3:
                    dve.wait_ge(mixed, at("mixed", "A1", j - s, 4 + s))
                    nc.vector.tensor_tensor(delta[:, s], delta[:, s], gates[:, s, :, D:2 * D], ALU.mult) \
                        .then_inc(mixed, 1)
                if n == 4:
                    dve.wait_ge(mixed, at("mixed", "A1", j - s, 6 + s))
                    nc.vector.tensor_tensor(delta[:, s], delta[:, s], cand[:, s], ALU.add).then_inc(mixed, 1)
                if n == 5:
                    dve.wait_ge(mixed, at("mixed", "A1", j - s, 8 + s))
                    nc.vector.tensor_tensor(x[:, blocks(j), :], x[:, blocks(j), :], delta[:, s], ALU.add) \
                        .then_inc(settled, 1)

            node_loop("A1", a1, 6)
            dve.wait_ge(settled, end("settled", "A1"))

            norm(2)

            def t2(n, j, s, i):
                dve.wait_ge(formed, at("formed", "T2", j - s, 2 + s))
                free_outs("T2", i, s)
                nc.vector.tensor_copy(outs[:, s, :], bank(2 + s)).then_inc(settled, 1)

            node_loop("T2", t2)
            edge_phase(2, interaction)

            def a2(n, j, s, i):
                dve.wait_ge(formed, at("formed", "A2", j))
                v = bank(2 + s)[:, 0:GB * D].rearrange("p (k c) -> p k c", k=GB)
                nc.vector.tensor_tensor(x[:, blocks(j), :], x[:, blocks(j), :], v, ALU.add).then_inc(settled, 1)

            node_loop("A2", a2)
            dve.wait_ge(settled, end("settled", "A2"))

            norm(3)
            edge_phase(3, plain(3, src_i))

            def a3(n, j, s, i):
                v = bank(2 + s).rearrange("p (k c) -> p k c", k=GB)
                if n == 0:
                    dve.wait_ge(shaped, at("shaped", "A3", j - s, s))
                    for k in range(GB):
                        ins = nc.vector.scalar_tensor_tensor(
                            out=hidn[:, s, k * H:(k + 1) * H], in0=v[:, k, :], scalar=cnt[:, bass.ds(j * GB + k, 1)],
                            in1=self_part[:, s, k * H:(k + 1) * H], op0=ALU.mult, op1=ALU.add)
                    ins.then_inc(mixed, 1)
                if n == 1:
                    dve.wait_ge(formed, at("formed", "A3", j - s, 2 + s))
                    free_outs("A3", i, s)
                    nc.vector.tensor_copy(outs[:, s, 0:GB * D].rearrange("p (k c) -> p k c", k=GB), v[:, :, 0:D])
                    nc.vector.tensor_tensor(x[:, blocks(j), :], x[:, blocks(j), :], v[:, :, D:2 * D], ALU.add) \
                        .then_inc(settled, 1)

            node_loop("A3", a3, 2)
            edge_phase(4, plain(4, src_i))

            def a4(n, j, s, i):
                dve.wait_ge(turned, at("turned", "A4", j))
                free_outs("A4", i, s)
                for k in range(GB):
                    ins = nc.vector.scalar_tensor_tensor(
                        out=outs[:, s, k * D:(k + 1) * D], in0=bank(s)[:, k * D:(k + 1) * D],
                        scalar=cnt[:, bass.ds(j * GB + k, 1)], in1=x[:, j * GB + k, :],
                        op0=ALU.mult, op1=ALU.add)
                ins.then_inc(settled, 1)

            node_loop("A4", a4)

        @block.scalar
        def _(act):
            for s_, n in ((softened1, 2 * RING), (softened2, 2 * RING), (sized1, RING), (hid_moved, RING), (inter_moved, RING),
                          (tanh_done, RING)):
                act.sem_inc(s_, n)
            P = passes_of(act)

            def norm(n):
                act.preload_act_table_set("sqrt_and_others")
                act.wait_ge(normed, 5 * n + 1)
                nc.scalar.activation(scr[:, :], h_flat, ACT.Square).then_inc(normed, 1)
                act.wait_ge(normed, 5 * n + 3)
                nc.scalar.activation(rstd[:, :], rstd[:, :], ACT.Sqrt, scale=1.0 / D, bias=eps_c[:, 0:1]) \
                    .then_inc(normed, 1)
                act.wait_ge(normed, 5 * n + 5)

            def node_loop(steps):
                with act.Fori(0, NG // 2) as i:
                    for step in steps:
                        for s in range(2):
                            step(i * 2 + s, s)

            def stage(loop, rows, with_h):
                def step(j, s):
                    n = ADDS["settled"][loop] - 1
                    act.wait_ge(settled, at("settled", loop, j, n, back=2))
                    act.sem_inc(act_turn, 1)
                    if rows:
                        ins = nc.scalar.activation(stage_a[0:rows, s, :], acc[0:rows, bass.ds(j * GN, GN)], ACT.Copy)
                    if with_h:
                        ins = nc.scalar.activation(stage_h[:, s], h[:, bass.ds(j * GB, GB), :], ACT.Copy)
                    ins.then_inc(staged, 1)
                return step

            def lift_h(loop):
                def step(j, s):
                    n = ADDS["turned"][loop]
                    act.wait_ge(turned, at("turned", loop, j - s, s))
                    nc.scalar.activation(hT[0:D, s, :], bank(s)[0:D, :], ACT.Copy).then_inc(lifted, 1)
                return step

            def sums_ready(e):
                act.wait_ge(agg_added, P * ((e + 1) * CH) + RING)

            norm(0)
            node_loop([stage("T0", 0, True), lift_h("T0")])

            act.preload_act_table_set("natural_log_exp_and_others")
            with act.Fori(0, P) as p:
                g = act.snap(p * CH)

                def soften(clipped, softened, buf):
                    def stage_(it, u, _):
                        act.wait_ge(clipped, done(g, it, u))
                        nc.scalar.activation(buf[:, u % 2, :], buf[:, u % 2, :], ACT.Exp).then_inc(softened, 1)
                        act.wait_ge(softened, done_of(2, g, it, u, 0))
                        nc.scalar.activation(buf[:, u % 2, :], buf[:, u % 2, :], ACT.Ln, bias=1.0).then_inc(softened, 1)
                    return stage_

                def soften_size(it, u, _):
                    act.wait_ge(mm1_done, done(g, it, u))
                    act.wait_ge(hid1_ready, done(g, it, u, 2))
                    nc.scalar.activation(soft1[:, u % 2, :], bank(u % 2), ACT.Abs).then_inc(sized1, 1)
                    act.wait_ge(sized1, done(g, it, u))
                    nc.scalar.activation(soft1[:, u % 2, :], soft1[:, u % 2, :], ACT.Exp, scale=-1.0) \
                        .then_inc(softened1, 1)
                    act.wait_ge(softened1, done_of(2, g, it, u, 0))
                    nc.scalar.activation(soft1[:, u % 2, :], soft1[:, u % 2, :], ACT.Ln, bias=1.0).then_inc(softened1, 1)

                def move(it, u, _):
                    act.wait_ge(hid_summed, done(g, it, u))
                    act.wait_ge(agg_done, done(g, it, u, 2))
                    nc.scalar.activation(moved[:, u % 2, :], bank(4 + u % 2)[:, 0:W], ACT.Copy).then_inc(hid_moved, 1)

                chunk_loop(act, [(2, soften_size), (4, soften(clipped2, softened2, soft2)),
                                 (5, move)])
            sums_ready(0)
            node_loop([stage("A0", D + 1, False)])

            norm(1)
            node_loop([stage("T1", 0, True), lift_h("T1")])
            act.preload_act_table_set("sigmoid_and_others")
            sums_ready(1)

            def sigmoid(j, s):
                act.wait_ge(formed, at("formed", "A1", j))
                v = ps[:, (2 + 2 * s) * 512:(4 + 2 * s) * 512].rearrange("p (k c) -> p k c", k=GB)
                nc.scalar.activation(gates[:, s], v[:, :, 0:2 * D], ACT.Sigmoid).then_inc(shaped, 1)

            def tanh(j, s):
                act.wait_ge(mixed, at("mixed", "A1", j - s, 2 + s))
                nc.scalar.activation(cand[:, s], cand[:, s], ACT.Tanh).then_inc(shaped, 1)

            node_loop([stage("A1", D, True), lift_h("A1"), sigmoid, tanh])

            norm(2)
            act.preload_act_table_set("exp_and_others")

            def tanh_pp(j, s):
                act.wait_ge(formed, at("formed", "T2", j - s, s))
                nc.scalar.activation(tT[0:D, s, :], bank(4 + s)[0:D, :], ACT.Tanh).then_inc(shaped, 1)

            node_loop([stage("T2", 0, True), lift_h("T2"), tanh_pp])
            with act.Fori(0, P) as p:
                g = act.snap(p * CH)
                ga = act.snap((P * 2 + p) * CH)

                def move_inter(it, u, _):
                    act.wait_ge(inter_done, done(g, it, u))
                    act.wait_ge(z_done, done_of(4, g, it, u, 3, 2 * 4))
                    nc.scalar.activation(inter[0:D, u % 2, :], bank(u % 2)[0:D, :], ACT.Copy)
                    nc.scalar.activation(inter[D:P128, u % 2, :], bank(u % 2)[0:D, :], ACT.Copy) \
                        .then_inc(inter_moved, 1)

                def tanh_ii(it, u, _):
                    act.wait_ge(pre_done, done(g, it, u))
                    act.wait_ge(agg_done, done(ga, it, u, 2))
                    nc.scalar.activation(tan[:, u % 2], bank(4 + u % 2)[:, 0:TL * D].rearrange("p (k c) -> p k c", k=TL),
                                         ACT.Tanh).then_inc(tanh_done, 1)

                chunk_loop(act, [(3, move_inter), (6, tanh_ii)])
            sums_ready(2)
            node_loop([stage("A2", D + 1, False)])

            norm(3)
            sums_ready(3)

            def own_part(j, s):
                act.wait_ge(formed, at("formed", "A3", j - s, s))
                nc.scalar.activation(self_part[:, s, :], bank(4 + s), ACT.Copy).then_inc(shaped, 1)

            def relu(j, s):
                act.wait_ge(mixed, at("mixed", "A3", j))
                nc.scalar.activation(hidn[:, s, :], hidn[:, s, :], ACT.Relu).then_inc(shaped, 1)

            def lift_hid(j, s):
                act.wait_ge(turned, at("turned", "A3", j - s, 2 + s))
                nc.scalar.activation(tT[:, s, :], bank(s), ACT.Copy).then_inc(lifted, 1)

            node_loop([stage("A3", D, True), lift_h("A3"), own_part, relu, lift_hid])
            sums_ready(4)
            node_loop([stage("A4", D, False)])

        @block.tensor
        def _(pe):
            for s_, n in ((agg_done, RING), (mm1_done, RING), (mm2_done, RING), (hid_summed, RING),
                          (inter_done, RING), (bas_spread, 4 * RING), (pre_done, RING)):
                pe.sem_inc(s_, n)
            mm = nc.tensor.matmul
            pe.wait_ge(loaded, ALL_LOADED)
            pe.wait_ge(consts, N_CONSTS)
            mm(bank(0)[0:D, 0:D], r_w1aT, r_w2, start=True, stop=True)
            mm(bank(0)[0:D, D:2 * D], r_w1bT, r_w2, start=True, stop=True).then_inc(folding, 1)
            pe.wait_ge(folded, 1)
            mm(bank(1)[0:D, 0:2 * D], r_pp2T, r_wab, start=True, stop=True)
            mm(bank(2)[0:1, 0:D], r_pp2b, r_wab[:, 0:D], start=True, stop=False)
            mm(bank(2)[0:1, 0:D], r_pp2b, r_wab[:, D:2 * D], start=False, stop=False)
            mm(bank(2)[0:1, 0:D], r_pib1, r_w2, start=False, stop=False)
            mm(bank(2)[0:1, 0:D], ones[0:1, 0:1], r_pib2, start=False, stop=True)
            for j in range(4):
                last = mm(bank(3)[:, j * D:(j + 1) * D], r_w3[:, j * P128:(j + 1) * P128], r_iw1, start=True, stop=True)
            last.then_inc(folding, 1)
            pe.wait_ge(bias_rt, 64)
            P = passes_of(pe)

            def node_loop(steps):
                with pe.Fori(0, NG // 2) as i:
                    for step in steps:
                        for s in range(2):
                            step(i * 2 + s, s)

            def turn_h(loop):
                def step(j, s):
                    pe.wait_ge(staged, at("staged", loop, j))
                    pe.sem_inc(pe_turn, 1)
                    for k in range(GB):
                        last = nc.tensor.transpose(bank(s)[0:D, k * P128:(k + 1) * P128], stage_h[:, s, k, :], ident[:, :])
                    last.then_inc(turned, 1)
                return step

            def turn_acc(loop, rows, step_cols):
                def step(j, s):
                    pe.wait_ge(staged, at("staged", loop, j))
                    pe.sem_inc(pe_turn, 1)
                    for k in range(GB):
                        last = nc.tensor.transpose(bank(s)[:, k * step_cols:k * step_cols + rows],
                                                   stage_a[0:rows, s, k * P128:(k + 1) * P128], ident[0:rows, 0:rows])
                    last.then_inc(turned, 1)
                return step

            def sum_stage(e, p, width, values, n_values, banks, summed=agg_done):
                ga = pe.snap((P * e + p) * CH)

                def stage(it, u, _):
                    n_values(it, u)
                    pe.wait_ge(sel_built, done(ga, it, u))
                    if summed is agg_done:
                        pe.wait_ge(agg_added, done(ga, it, u, len(banks)))
                    for k in range(TL):
                        last = mm(bank(banks[u % len(banks)])[0:width, 0:W], values(u)[:, k, :], sel[:, u, k, :],
                                  start=k == 0, stop=k == TL - 1)
                    last.then_inc(summed, 1)
                return stage

            def rows_g(j, s):
                pe.wait_ge(lifted, at("lifted", "T0", j))
                for k in range(GB):
                    last = mm(bank(2 + s)[:, k * H:(k + 1) * H], hT[:, s, k * P128:(k + 1) * P128], w_l0n[:, :],
                              start=True, stop=True)
                last.then_inc(formed, 1)

            node_loop([turn_h("T0"), rows_g])
            with pe.Fori(0, P) as p:
                g = pe.snap(p * CH)

                def hid2_here(it, u):
                    pe.wait_ge(hid2_ready, done(g, it, u))

                def mm2(it, u, _):
                    pe.wait_ge(hid1_ready, done(g, it, u))
                    pe.wait_ge(hid2_ready, done(g, it, u, 2))
                    out_ = bank(2 + u % 2).rearrange("p (k c) -> p k c", k=TL)
                    mm(out_, ones_b[:, :], bpart[:, 0:H].unsqueeze(1).to_broadcast([3, TL, H]), start=True, stop=False)
                    for k in range(TL):
                        last = mm(out_[:, k, :], hid1[:, u % 2, k * P128:(k + 1) * P128], w_l0m[:, :],
                                  start=False, stop=k == TL - 1)
                    last.then_inc(mm2_done, 1)

                def mm1(it, u, _):
                    pe.wait_ge(selT_built, done(g, it, u))
                    pe.wait_ge(hid1_ready, done(g, it, u, 2))
                    mm(bank(u % 2), win[:, u, :], mov[:, u, :], start=True, stop=True).then_inc(mm1_done, 1)

                def to_acc(it, u, _):
                    pe.wait_ge(hid_moved, done(g, it, u))
                    pe.wait_ge(agg_added, done(g, it, u, 2))
                    out_ = bank(6 + u % 2)[0:D + 1, 0:W]
                    for k in range(TL):
                        mm(out_, b_l0o[:, :], sel[:, u, k, :], start=k == 0, stop=False)
                    mm(out_, w_l0o[:, :], moved[:, u % 2, :], start=False, stop=True).then_inc(agg_done, 1)

                chunk_loop(pe, [
                    (5, sum_stage(0, p, H, lambda u: hid2[:, u % 2, :].rearrange("p (k c) -> p k c", k=TL),
                                  hid2_here, (4, 5), hid_summed)),
                    (3, mm2), (1, mm1), (6, to_acc)])
            node_loop([turn_acc("A0", D + 1, P128)])

            def gathered_here(e, p):
                gg = pe.snap((P * GATHER[e] + p) * ITERS)
                return lambda it, u: pe.wait_ge(gathered[u], (gg + it) * (16 * TL) + 16 * TL)

            def plain(e):
                with pe.Fori(0, P) as p:
                    chunk_loop(pe, [(0, sum_stage(e, p, D, lambda u: gat[:, u], gathered_here(e, p), (4, 5, 6, 7)))])

            def rows_msg(j, s):
                pe.wait_ge(lifted, at("lifted", "T1", j))
                for k in range(GB):
                    pe.wait_ge(settled, at("settled", "T1", j, k, back=1))
                    mm(bank(2 + k), hT[0:D, s, k * P128:(k + 1) * P128], w_typ[:, :], start=True, stop=True) \
                        .then_inc(formed, 1)

            node_loop([turn_h("T1"), rows_msg])
            plain(1)

            def gru(j, s):
                pe.wait_ge(lifted, at("lifted", "A1", j))
                for k in range(GB):
                    out_ = ps[:, (2 + 2 * s) * 512 + k * 4 * D:(2 + 2 * s) * 512 + (k + 1) * 4 * D]
                    mm(out_, stage_a[0:D, s, k * P128:(k + 1) * P128], w_ih[:, :], start=True, stop=False)
                    last = mm(out_, hT[:, s, k * P128:(k + 1) * P128], w_hh[:, :], start=False, stop=True)
                last.then_inc(formed, 1)

            node_loop([turn_h("A1"), gru])

            def pp1(j, s):
                pe.wait_ge(lifted, at("lifted", "T2", j))
                mm(bank(4 + s)[0:D, :], w_pp1[:, :], hT[:, s, :], start=True, stop=True).then_inc(formed, 1)

            def rows_uv(j, s):
                pe.wait_ge(shaped, at("shaped", "T2", j))
                for k in range(GB):
                    last = mm(bank(2 + s)[:, k * H:(k + 1) * H], tT[0:D + 1, s, k * P128:(k + 1) * P128], w_uv[:, :],
                              start=True, stop=True)
                last.then_inc(formed, 1)

            node_loop([turn_h("T2"), pp1, rows_uv])
            with pe.Fori(0, P) as p:
                g = pe.snap(p * CH)
                here = gathered_here(2, p)

                def inter_stage(it, u, _):
                    pe.wait_ge(selT_built, done(g + P * CH, it, u))
                    here(it, u)
                    pe.wait_ge(inter_moved, done(g, it, u, 2))
                    for k in range(TL):
                        cols = slice(k * P128, (k + 1) * P128)
                        mm(bank(u % 2)[0:D, cols], gat[:, u, k, :], ident[:, :], start=True, stop=False)
                        last = mm(bank(u % 2)[0:D, cols], win[0:D, u, 0:D], mov[0:D, u, cols], start=False, stop=True)
                    last.then_inc(inter_done, 1)

                def spread(it, u, j):
                    pe.wait_ge(z_done, done_of(4, g, it, u, j, 2))
                    mm(bank(2 + j % 2), pair[:, j, :], bas[:, u, :], start=True, stop=True).then_inc(bas_spread, 1)

                def weigh(it, u, j):
                    out_ = bank(4 + u % 2)[:, 0:TL * D].rearrange("p (k c) -> p k c", k=TL)
                    if j == 0:
                        pe.wait_ge(tanh_done, done(g, it, u, 2))
                        mm(out_, ones_b[:, :], bpart[:, H:H + D].unsqueeze(1).to_broadcast([3, TL, D]),
                           start=True, stop=False)
                    pe.wait_ge(z_done, done_of(4, g, it, u, j))
                    for k in range(TL):
                        last = mm(out_[:, k, :], zed[:, u % 2, j, k * P128:(k + 1) * P128], w_bas[:, j, :],
                                  start=False, stop=j == 3 and k == TL - 1)
                    if j == 3:
                        last.then_inc(pre_done, 1)

                def tan_here(it, u):
                    pe.wait_ge(tanh_done, done(g, it, u))

                chunk_loop(pe, [
                    (3, inter_stage),
                    (4, lambda it, u, _: (spread(it, u, 0), spread(it, u, 1))),
                    (5, lambda it, u, _: weigh(it, u, 0)), (4, lambda it, u, _: spread(it, u, 2)),
                    (5, lambda it, u, _: weigh(it, u, 1)), (4, lambda it, u, _: spread(it, u, 3)),
                    (5, lambda it, u, _: (weigh(it, u, 2), weigh(it, u, 3))),
                    (7, sum_stage(2, p, D, lambda u: tan[:, u % 2], tan_here, (6, 7)))])

            def result2(j, s):
                pe.wait_ge(staged, at("staged", "A2", j))
                for k in range(GB):
                    last = mm(bank(2 + s)[:, k * D:(k + 1) * D], stage_a[0:D + 1, s, k * P128:(k + 1) * P128],
                              w_ii2[:, :], start=True, stop=True)
                last.then_inc(formed, 1)

            node_loop([result2])

            plain(3)

            def turn3(j, s):
                pe.wait_ge(staged, at("staged", "A3", j))
                pe.sem_inc(pe_turn, 1)
                for k in range(GB):
                    last = nc.tensor.transpose(bank(s)[0:D, k * P128:(k + 1) * P128], stage_h[:, s, k, :], ident[:, :])
                last.then_inc(turned, 1)

            def conv1(j, s):
                pe.wait_ge(lifted, at("lifted", "A3", j - s, s))
                for k in range(GB):
                    cols = slice(k * P128, (k + 1) * P128)
                    mm(bank(2 + s)[:, cols], stage_a[0:D, s, cols], w_c1l[:, :], start=True, stop=True)
                    last = mm(bank(4 + s)[:, cols], hT[:, s, cols], w_c1r[:, :], start=True, stop=True)
                last.then_inc(formed, 1)

            def turn_hid(j, s):
                pe.wait_ge(shaped, at("shaped", "A3", j - s, 2 + s))
                pe.sem_inc(pe_turn, 1)
                for k in range(GB):
                    cols = slice(k * P128, (k + 1) * P128)
                    last = nc.tensor.transpose(bank(s)[:, cols], hidn[:, s, cols], ident[:, :])
                last.then_inc(turned, 1)

            def conv2(j, s):
                pe.wait_ge(lifted, at("lifted", "A3", j - s, 2 + s))
                for k in range(GB):
                    cols = slice(k * P128, (k + 1) * P128)
                    mm(bank(2 + s)[:, cols], tT[:, s, cols], w_c2[:, :], start=True, stop=False)
                    last = mm(bank(2 + s)[:, cols], ones[0:1, :], b_c2[:, :], start=False, stop=True)
                last.then_inc(formed, 1)

            node_loop([turn3, conv1, turn_hid, conv2])
            plain(4)
            node_loop([turn_acc("A4", D, D)])


def lay_out(i, RNG=RING):
    import numpy as np
    a = {k: np.asarray(v) for k, v in i.items()}
    n = a["x"].shape[0]
    e = a["src"].shape[0]
    chunks = -(-e // CE)
    chunks += -chunks % RNG
    ep = chunks * CE
    npn = -(-(n + W) // (2 * GN)) * (2 * GN)

    def pad(v, fill):
        return np.concatenate([v, np.full((ep - e,) + v.shape[1:], fill, v.dtype)])

    def edge_major(v):
        return np.ascontiguousarray(v.reshape(chunks * TL, P128).T)

    def row(v):
        return np.ascontiguousarray(v.reshape(1, -1))

    def col(v):
        return np.ascontiguousarray(v.reshape(-1, 1))

    src, dst, typ = pad(a["src"], 0), pad(a["dst"], -1), pad(a["edge_type_8"], 0)
    first = np.concatenate([a["dst"][::CE], np.zeros(chunks - len(a["dst"][::CE]), a["dst"].dtype)])
    g = dict(
        x=np.concatenate([a["x"], np.zeros((npn - n, D), a["x"].dtype)]),
        src_em=edge_major(src), dst_em=edge_major(dst), typ_em=edge_major(typ),
        dst_row=row(dst), dst_first=row(first),
        ea64_T=np.ascontiguousarray(pad(a["edge_attr_64"], 0).T),
        ea8_T=np.ascontiguousarray(pad(a["edge_attr_8"], 0).T).reshape(P128, -1),
        L0_W1=a["L0_gnn_W1"], L0_b1=row(a["L0_gnn_b1"]), L0_W2=a["L0_gnn_W2"], L0_b2=row(a["L0_gnn_b2"]),
        L0_W3=a["L0_gnn_W3"], L0_b3=row(a["L0_gnn_b3"]),
        A_T=np.ascontiguousarray(a["L1_gnn_edge_matrix"].reshape(NT, D, D).transpose(2, 0, 1)).reshape(D, NT * D),
        w_ih_T=np.ascontiguousarray(a["L1_gnn_w_ih"].T), w_hh_T=np.ascontiguousarray(a["L1_gnn_w_hh"].T),
        b_ih=row(a["L1_gnn_b_ih"]), b_hh=row(a["L1_gnn_b_hh"]),
        pp_W1=a["L2_gnn_pp_W1"], pp_b1=row(a["L2_gnn_pp_b1"]), pp_W2_T=np.ascontiguousarray(a["L2_gnn_pp_W2"].T),
        pp_b2=col(a["L2_gnn_pp_b2"]), pi_W1_T=np.ascontiguousarray(a["L2_gnn_pi_W1"].T), pi_b1=col(a["L2_gnn_pi_b1"]),
        pi_W2=a["L2_gnn_pi_W2"], pi_b2=row(a["L2_gnn_pi_b2"]),
        pi_W3_T=np.ascontiguousarray(a["L2_gnn_pi_W3"].reshape(D, D, NBAS).transpose(1, 2, 0)).reshape(D, NBAS * D),
        ii_W1=a["L2_gnn_ii_W1"], ii_b1=row(a["L2_gnn_ii_b1"]), ii_W2=a["L2_gnn_ii_W2"], ii_b2=row(a["L2_gnn_ii_b2"]),
        c1_Wl=a["L3_gnn_W1_l"], c1_Wr=a["L3_gnn_W1_r"], c1_b=row(a["L3_gnn_b1"]),
        c2_Wl=a["L3_gnn_W2_l"], c2_Wr=a["L3_gnn_W2_r"], c2_b=row(a["L3_gnn_b2"]),
    )
    return g, n, chunks, npn


def kernel(**inputs):
    import concourse.bacc as _bacc
    from concourse.bass_utils import run_bass_kernel_spmd as _run

    laid, n, chunks, npn = lay_out(inputs)
    nc = _bacc.Bacc("TRN2", target_bir_lowering=False, num_devices=1)
    arrays, args = {}, {}
    for name, a in laid.items():
        arrays[f"in_{name}"] = a
        args[name] = nc.dram_tensor(f"in_{name}", a.shape, mybir.dt.from_np(a.dtype), kind="ExternalInput").ap()
    out = nc.dram_tensor("out_nodes", [npn, D], F32, kind="ExternalOutput").ap()
    build_gnn(nc, args, out, n, chunks, npn)
    r = _run(nc, [arrays], core_ids=[0])
    return r.results[0]["out_nodes"][:n]
```
